# Optimizing a Trainium2 kernel written in Bass

```python
import numpy as np
import jax
import jax.numpy as jnp

def _softmax(x, axis=-1):
    return jax.nn.softmax(x, axis=axis)

def _gelu(x):
    return jax.nn.gelu(x, approximate=True)

def _silu(x):
    return jax.nn.silu(x)

def _sigmoid(x):
    return jax.nn.sigmoid(x)

def _layernorm(x, axis=-1, eps=1e-05):
    m = jnp.mean(x, axis=axis, keepdims=True)
    v = jnp.var(x, axis=axis, keepdims=True)
    return (x - m) / jnp.sqrt(v + eps)

def _scatter_add(tgt, idx, src, axis=0):
    return tgt.at[idx].add(src)

def _segment_sum(src, seg, n):
    return jax.ops.segment_sum(src, seg, n)
kernel_name = 'mk_prb_d1_jaxref_r4_ea524c'

def setup_inputs(seed: int=0):
    np.random.seed(seed)
    _w = jnp.asarray

    def _L0_attn_setup():
        import jax, jax.numpy as jnp
        import numpy as np
        B, S, D = (4, 512, 256)
        DK, DV = (256, 256)
        key = jax.random.key(seed)
        ks = jax.random.split(key, 5)
        x = jax.random.normal(ks[0], (B, S, D), dtype=jnp.float32)
        scale = 1.0 / np.sqrt(D)
        Wq = jax.random.normal(ks[1], (D, DK), dtype=jnp.float32) * scale
        Wk = jax.random.normal(ks[2], (D, DK), dtype=jnp.float32) * scale
        Wv = jax.random.normal(ks[3], (D, DV), dtype=jnp.float32) * scale
        Wo = jax.random.normal(ks[4], (DV, DV), dtype=jnp.float32) * (1.0 / np.sqrt(DV))
        return {'x': x, 'Wq': Wq, 'Wk': Wk, 'Wv': Wv, 'Wo': Wo}
    _L0_attn_in = _L0_attn_setup()

    def _L0_ffn_setup():
        import jax, jax.numpy as jnp
        import numpy as np
        D_IN, D_HID = (256, 1024)

        def _ternary(key, shape):
            return jax.random.randint(key, shape, -1, 2).astype(jnp.float32)

        def _tlin(x, w, s):
            return jnp.einsum('bsi,oi->bso', x, w) * s
        key = jax.random.key(seed)
        ks = jax.random.split(key, 12)
        inv = lambda fan: 1.0 / np.sqrt(fan).astype(np.float32)
        return {'x': jax.random.normal(ks[0], (4, 512, D_IN), dtype=jnp.float32), 'w1_w': _ternary(ks[1], (D_HID, D_IN)), 'w1_s': jax.random.uniform(ks[2], (D_HID,), dtype=jnp.float32) * inv(D_IN), 'w2_w': _ternary(ks[3], (D_HID, D_IN)), 'w2_s': jax.random.uniform(ks[4], (D_HID,), dtype=jnp.float32) * inv(D_IN), 'h1_w': _ternary(ks[5], (D_HID, D_HID)), 'h1_s': jax.random.uniform(ks[6], (D_HID,), dtype=jnp.float32) * inv(D_HID), 'h2_w': _ternary(ks[7], (D_HID, D_HID)), 'h2_s': jax.random.uniform(ks[8], (D_HID,), dtype=jnp.float32) * inv(D_HID), 'w3_w': _ternary(ks[9], (D_IN, D_HID)), 'w3_s': jax.random.uniform(ks[10], (D_IN,), dtype=jnp.float32) * inv(D_HID)}
    _L0_ffn_in = _L0_ffn_setup()
    _d = {'L0_attn_x': _L0_attn_in['x'], 'L0_attn_Wq': _L0_attn_in['Wq'], 'L0_attn_Wk': _L0_attn_in['Wk'], 'L0_attn_Wv': _L0_attn_in['Wv'], 'L0_attn_Wo': _L0_attn_in['Wo'], 'L0_ffn_w1_w': _L0_ffn_in['w1_w'], 'L0_ffn_w1_s': _L0_ffn_in['w1_s'], 'L0_ffn_w2_w': _L0_ffn_in['w2_w'], 'L0_ffn_w2_s': _L0_ffn_in['w2_s'], 'L0_ffn_h1_w': _L0_ffn_in['h1_w'], 'L0_ffn_h1_s': _L0_ffn_in['h1_s'], 'L0_ffn_h2_w': _L0_ffn_in['h2_w'], 'L0_ffn_h2_s': _L0_ffn_in['h2_s'], 'L0_ffn_w3_w': _L0_ffn_in['w3_w'], 'L0_ffn_w3_s': _L0_ffn_in['w3_s']}
    _x0 = _d['L0_attn_x']
    _d['L0_attn_x'] = jax.random.normal(jax.random.fold_in(jax.random.key(seed), 1), (2, 2048, 256), dtype=_x0.dtype)
    del _x0
    return _d

def reference(L0_attn_x, L0_attn_Wq, L0_attn_Wk, L0_attn_Wv, L0_attn_Wo, L0_ffn_w1_w, L0_ffn_w1_s, L0_ffn_w2_w, L0_ffn_w2_s, L0_ffn_h1_w, L0_ffn_h1_s, L0_ffn_h2_w, L0_ffn_h2_s, L0_ffn_w3_w, L0_ffn_w3_s):

    def _L0_attn_ref(x, Wq, Wk, Wv, Wo):
        import jax, jax.numpy as jnp
        import numpy as np
        B, S, D = (4, 512, 256)
        DK, DV = (256, 256)
        dim_k = Wq.shape[1]
        q = x @ Wq
        k = x @ Wk
        v = x @ Wv
        scores = jnp.einsum('bsd,btd->bst', q, k)
        m_inf = -jnp.finfo(scores.dtype).max
        causal_mask = jnp.triu(jnp.ones((q.shape[1], q.shape[1]), dtype=bool), k=1)
        scores = jnp.where(causal_mask[None, :, :], m_inf, scores)
        attn = jax.nn.softmax(scores * dim_k ** (-0.5), axis=-1)
        out = jnp.einsum('bst,btv->bsv', attn, v) @ Wo
        return out

    def _L0_ffn_ref(x, w1_w, w1_s, w2_w, w2_s, h1_w, h1_s, h2_w, h2_s, w3_w, w3_s):
        import jax, jax.numpy as jnp
        import numpy as np
        D_IN, D_HID = (256, 1024)

        def _ternary(key, shape):
            return jax.random.randint(key, shape, -1, 2).astype(jnp.float32)

        def _tlin(x, w, s):
            return jnp.einsum('bsi,oi->bso', x, w) * s
        h = jax.nn.silu(_tlin(x, w1_w, w1_s)) * _tlin(x, w2_w, w2_s)
        h = jax.nn.gelu(_tlin(h, h1_w, h1_s), approximate=False)
        h = jax.nn.gelu(_tlin(h, h2_w, h2_s), approximate=False)
        return _tlin(h, w3_w, w3_s)
    x = L0_attn_x
    xn = _layernorm(x, axis=-1)
    x = x + _L0_attn_ref(xn, L0_attn_Wq, L0_attn_Wk, L0_attn_Wv, L0_attn_Wo) + _L0_ffn_ref(xn, L0_ffn_w1_w, L0_ffn_w1_s, L0_ffn_w2_w, L0_ffn_w2_s, L0_ffn_h1_w, L0_ffn_h1_s, L0_ffn_h2_w, L0_ffn_h2_s, L0_ffn_w3_w, L0_ffn_w3_s)
    return x

_drawn_inputs = setup_inputs


def setup_inputs(seed=0):
    import zlib

    import numpy as np

    out = dict(_drawn_inputs(seed))
    spreads = {}
    factors = {}
    for name, (base, spread) in spreads.items():
        noise = np.random.default_rng([zlib.crc32(name.encode()), seed]).standard_normal(out[name].shape)
        drawn = base * np.exp(spread * noise) if base else spread * noise
        out[name] = jnp.asarray(drawn.astype(out[name].dtype))
    for name, factor in factors.items():
        out[name] = (out[name] * factor).astype(out[name].dtype)
    return out
```

```python
from contextlib import ExitStack

import concourse.bass as bass
from concourse import mybir

F32 = mybir.dt.float32
F32R = mybir.dt.float32r
BF16 = mybir.dt.bfloat16
I32 = mybir.dt.int32
U32 = mybir.dt.uint32
ALU = mybir.AluOpType
ACT = mybir.ActivationFunctionType
X = mybir.AxisListType.X

P = 128
BANK = 512
B, S, D = 2, 2048, 256
HID = 1024
KD = D // P
KH = HID // P
GROUP = BANK
GROUPS = S // GROUP
TILES = S // P
PER = GROUP // P
CHUNKS = B * GROUPS
LN_EPS = 1e-5
MASKED = -3.0e38
LOW_BITS = 12

MISC_BANKS = (4, 5, 6)
OUT_BANK = 7
PT_SLOTS = 4
RES_SLOTS = 4

W1, W2, H1, H2, W3 = 0, KD * HID, 2 * KD * HID, 2 * KD * HID + KH * HID, 2 * KD * HID + 2 * KH * HID
WCOLS = W3 + KH * D
LOAD = 2048
LOADS = WCOLS // LOAD
CHECK = 512


def pieces(t):
    return t // PER + 1


def width(t, c):
    return BANK if c < t // PER else (t % PER + 1) * P


def piece(t, c=0):
    return sum(pieces(i) for i in range(t)) + c


PIECES = piece(TILES)


def misc_order():
    order = [("xT", 0, 0), ("xT", 0, 1), ("y", 0, 0), ("y", 0, 1), ("v", 0, 0), ("v", 0, 1)]
    for t in range(TILES):
        g = t // PER + 1
        order += [("pT", t, c) for c in range(min(2, pieces(t)))]
        if g < GROUPS and t % PER == 2:
            order += [("xT", g, 0), ("xT", g, 1)]
        if g < GROUPS and t % PER == 3:
            order += [("y", g, 0), ("y", g, 1), ("v", g, 0), ("v", g, 1)]
        order += [("pT", t, c) for c in range(2, pieces(t))]
    return {use: n for n, use in enumerate(order)}


MISC = misc_order()
MISC0 = 2


def misc_bank(use):
    return MISC_BANKS[MISC[use] % len(MISC_BANKS)]


def misc_count(b, use):
    return b * len(MISC) + (MISC0 + MISC[use] + 1)


def build(nc, x, wqT, wkT, wvT, wo, ffn_w, s1, s2, sh1, sh2, s3, out):
    xf = x.rearrange("b s d -> (b s) d")
    outf = out.rearrange("b s d -> (b s) d")
    raw_w = nc.dram_tensor("raw_w", [LOADS, P, LOAD], F32, kind="Internal").ap()
    xn_dram = nc.dram_tensor("xn_dram", [CHUNKS * P, 2 * KD * GROUP], F32, kind="Internal").ap()
    res_dram = nc.dram_tensor("res_dram", [B * S, D], F32, kind="Internal").ap()

    with ExitStack() as ctx:
        def sb(name, shape, dt):
            return ctx.enter_context(nc.sbuf_tensor(name, shape, dt))

        def sem(name):
            return ctx.enter_context(nc.semaphore(name))

        weights = sb("weights", [P, WCOLS], F32R)
        XT, VV, YT, PT = 0, 2 * KD * S, 2 * KD * S + 2 * TILES * D, 2 * KD * S + 2 * TILES * D + 2 * KD * GROUP
        REGION = PT + PT_SLOTS * 2 * BANK
        region = sb("region", [P, REGION], F32R)
        xnT = region[:, XT:VV].rearrange("p (g l k n) -> p g l k n", g=GROUPS, l=2, k=KD)
        val = region[:, VV:YT].rearrange("p (t l n) -> p t l n", t=TILES, l=2)
        yT = region[:, YT:PT].rearrange("p (l k n) -> p l k n", l=2, k=KD)
        probsT = region[:, PT:REGION].rearrange("p (s l n) -> p s l n", s=PT_SLOTS, l=2)
        CHUNK_COLS, HID_COLS = 2 * KD * GROUP, 2 * KH * GROUP
        chunk_x = region[:, 0:2 * CHUNK_COLS].rearrange("p (u l k n) -> p u l k n", u=2, l=2, k=KD)
        hidden = [region[:, 2 * CHUNK_COLS + i * HID_COLS:2 * CHUNK_COLS + (i + 1) * HID_COLS]
                  .rearrange("p (k l n) -> p k l n", k=KH, l=2) for i in range(2)]
        proj = sb("proj", [P, 2, 2, KD, D], F32R)
        probs = sb("probs", [P, S], F32)
        attn_w = probs[:, :].rearrange("p (w k n) -> p w k n", w=4, k=KD)
        act_out = probs[:, :].rearrange("p (u n) -> p u n", u=4)
        xs = sb("xs", [P, PER, D], F32)
        gated = xs[:, :, :].rearrange("p r n -> p (r n)").rearrange("p (u n) -> p u n", u=2)
        res = sb("res", [P, RES_SLOTS, D], F32)
        ident = sb("ident", [P, P], F32)
        ident_h = sb("ident_h", [P, P], BF16)
        mask = sb("mask", [P, P], BF16)
        low = sb("low", [P, CHECK], U32)
        low_shift = sb("low_shift", [P, 1], U32)
        low_sum = sb("low_sum", [P, CHECK], U32)
        low_any = sb("low_any", [P, 1], F32)
        ones = sb("ones", [P, 1], F32)
        inexact = sb("inexact", [1, 1], I32)
        scale_in = sb("scale_in", [P, 2, KH], F32)
        scale_hid = sb("scale_hid", [P, 2, KH], F32)
        scale_out = sb("scale_out", [P, D], F32)
        stats = sb("stats", [P, PER, 6], F32)
        halves = sb("halves", [P, 4, PER], F32)
        mean = sb("mean", [P, PER], F32)
        d_var = sb("d_var", [P, PER], F32)
        log_var = sb("log_var", [P, PER], F32)
        newton = sb("newton", [P, 3, PER], F32)
        rstd0 = sb("rstd0", [P, PER], F32)
        rstd = sb("rstd", [P, PER], F32)
        piece_max = sb("piece_max", [P, 4], F32)
        neg_max = sb("neg_max", [P, 2], F32)
        piece_sum = sb("piece_sum", [P, 2, 4], F32)
        row_sum = sb("row_sum", [P, 1], F32)
        row_inv = sb("row_inv", [P, 1], F32)

        ps = ctx.enter_context(nc.psum_tensor("ps", [P, 8, BANK], F32))

        attn_w_loaded = sem("attn_w_loaded")
        consts_ready = sem("consts_ready")
        pool_fill = sem("pool_fill")
        scales_loaded = sem("scales_loaded")
        raw_copied = sem("raw_copied")
        weights_loaded = sem("weights_loaded")
        x_loaded = sem("x_loaded")
        stats_done = sem("stats_done")
        moment_step = sem("moment_step")
        moments_done = sem("moments_done")
        log_done = sem("log_done")
        rstd0_done = sem("rstd0_done")
        newton_step = sem("newton_step")
        xn_ready = sem("xn_ready")
        misc_full = sem("misc_full")
        misc_hi = sem("misc_hi")
        misc_empty = sem("misc_empty")
        scores_full = sem("scores_full")
        pieces_max_done = sem("pieces_max_done")
        max_ready = sem("max_ready")
        probs_ready = sem("probs_ready")
        out_full = sem("out_full")
        norm_step = sem("norm_step")
        out_evacuated = sem("out_evacuated")
        res_loaded = [sem(f"res_loaded{i}") for i in range(RES_SLOTS)]
        res_stored = [sem(f"res_stored{i}") for i in range(RES_SLOTS)]
        xn_stored = sem("xn_stored")
        low_step = sem("low_step")
        low_ready = sem("low_ready")
        low_summed = sem("low_summed")
        inexact_ready = sem("inexact_ready")
        chunk_loaded = [sem(f"chunk_loaded{i}") for i in range(2)]
        res_chunk_loaded = sem("res_chunk_loaded")
        pre_full = sem("pre_full")
        act_done = sem("act_done")
        gate_done = sem("gate_done")
        hi_done = sem("hi_done")
        hid_ready = sem("hid_ready")
        ffn_full = sem("ffn_full")
        ffn_scaled = sem("ffn_scaled")
        out_stored = sem("out_stored")

        block = ctx.enter_context(nc.Block())

        def rows(first, n):
            return bass.ds(first, n)

        def in_range(first, most):
            return nc.s_assert_within(first, 0, most, skip_runtime_bounds_check_because="the branch leaves out the last")

        def group_rows(dram, first):
            return dram[rows(first, GROUP), :].rearrange("(r p) d -> p r d", p=P)

        @block.sync
        def _(sp):
            sp.dma_start(xs[:], group_rows(xf, 0)).then_inc(x_loaded, 16)
            for i, w in enumerate((wqT, wkT, wvT, wo)):
                sp.dma_start(attn_w[:, i], w.rearrange("(k p) n -> p k n", p=P)).then_inc(attn_w_loaded, 16)
            for i, s in enumerate((s1, s2)):
                sp.dma_start(scale_in[:, i], s).then_inc(scales_loaded, 16)
            for i, s in enumerate((sh1, sh2)):
                sp.dma_start(scale_hid[:, i], s).then_inc(scales_loaded, 16)
            sp.dma_start(scale_out[:], s3.partition_broadcast(P)).then_inc(scales_loaded, 16)

            def load_res(first, t):
                sp.dma_start(res[:, t % RES_SLOTS], xf[rows(first + t * P, P), :]).then_inc(res_loaded[t % RES_SLOTS], 16)

            for t in range(RES_SLOTS - 1):
                load_res(0, t)
            with sp.Fori(0, B) as b:
                def load_x(g, first):
                    sp.wait_ge(misc_full, misc_count(b, ("xT", g, 1)))
                    sp.dma_start(xs[:], group_rows(xf, first)).then_inc(x_loaded, 16)

                def store_xn(g):
                    sp.wait_ge(misc_empty, misc_count(b, ("xT", g, 1)))
                    sp.dma_start(xn_dram[rows(b * (GROUPS * P) + g * P, P), :],
                                 xnT[:, g].rearrange("p l k n -> p (l k n)").bitcast(F32)
                                 ).then_inc(xn_stored, 16)

                for t in range(TILES):
                    g = t // PER
                    if t == 0:
                        load_x(0, b * S + GROUP)
                    if t % PER == 0:
                        store_xn(g)
                    sp.wait_ge(out_evacuated, b * TILES + t + 2)
                    sp.dma_start(res_dram[rows(b * S + t * P, P), :], res[:, t % RES_SLOTS]
                                 ).then_inc(res_stored[t % RES_SLOTS], 16)
                    if t % PER == 2:
                        if g + 2 < GROUPS:
                            load_x(g + 1, b * S + (g + 2) * GROUP)
                        elif g + 2 == GROUPS:
                            with sp.If(b < B - 1):
                                load_x(g + 1, in_range((b + 1) * S, (B - 1) * S))
                    n = t + RES_SLOTS - 1
                    if n < TILES:
                        if n >= RES_SLOTS:
                            sp.wait_ge(res_stored[n % RES_SLOTS], b * (16 * PER) + 16 * (n // RES_SLOTS))
                        load_res(b * S, n)
                with sp.If(b < B - 1):
                    for t in range(RES_SLOTS - 1):
                        sp.wait_ge(res_stored[t], b * (16 * PER) + 16 * PER)
                        load_res(in_range((b + 1) * S, (B - 1) * S), t)

            def load_res_chunk(first):
                sp.dma_start(res[:], group_rows(res_dram, first)).then_inc(res_chunk_loaded, 16)

            for i in range(RES_SLOTS):
                sp.wait_ge(res_stored[i], B * PER * 16)
            load_res_chunk(0)
            with sp.Fori(0, CHUNKS // 2) as it:
                for u in range(2):
                    c = it * 2 + u
                    with sp.If(it < CHUNKS // 2 - 1):
                        sp.wait_ge(pre_full, c * 32 + 16)
                        sp.dma_start(chunk_x[:, u].rearrange("p l k n -> p (l k n)").bitcast(F32),
                                     xn_dram[rows(in_range(it * (2 * P) + (u + 2) * P, (CHUNKS - 1) * P), P), :]
                                     ).then_inc(chunk_loaded[u], 16)
                    sp.wait_ge(out_evacuated, c * PER + (B * TILES + 1 + PER))
                    sp.dma_start(group_rows(outf, it * (2 * GROUP) + u * GROUP), res[:]).then_inc(out_stored, 16)
                    if u == 0:
                        sp.wait_ge(out_stored, c * 16 + 16)
                        load_res_chunk(it * (2 * GROUP) + GROUP)
                    else:
                        with sp.If(it < CHUNKS // 2 - 1):
                            sp.wait_ge(out_stored, c * 16 + 16)
                            load_res_chunk(in_range((it + 1) * (2 * GROUP), (CHUNKS - 2) * GROUP))
            sp.wait_ge(out_stored, CHUNKS * 16)

        @block.gpsimd
        def _(pool):
            pool.memset(ident[:], 0.0).then_inc(pool_fill, 1)
            pool.memset(ident_h[:], 0.0).then_inc(pool_fill, 1)
            pool.memset(mask[:], 0.0).then_inc(pool_fill, 1)
            pool.memset(ones[:], 1.0).then_inc(consts_ready, 1)
            pool.wait_ge(pool_fill, 3)
            for i in (ident, ident_h):
                pool.affine_select(out=i[:], in_=i[:], pattern=[[-1, P]], compare_op=ALU.not_equal, fill=1.0,
                                   base=0, channel_multiplier=1).then_inc(consts_ready, 1)
            pool.affine_select(out=mask[:], in_=mask[:], pattern=[[-1, P]], compare_op=ALU.is_ge, fill=MASKED,
                               base=0, channel_multiplier=1).then_inc(consts_ready, 1)
            pool.memset(low_shift[:], 1 << (32 - LOW_BITS)).then_inc(low_step, 1)
            pool.memset(low_sum[:], 0).then_inc(low_step, 1)
            pool.wait_ge(x_loaded, 16)
            pool.wait_ge(attn_w_loaded, 64)
            pool.dma_start(raw_w[0], ffn_w[0]).then_inc(raw_copied, 16)
            for n in range(LOADS):
                pool.wait_ge(raw_copied, 16 * (n + 1))
                pool.dma_start(weights[:, n * LOAD:(n + 1) * LOAD].bitcast(F32), raw_w[n]).then_inc(weights_loaded, 16)
                if n + 1 < LOADS:
                    pool.dma_start(raw_w[n + 1], ffn_w[n + 1]).then_inc(raw_copied, 16)
                pool.wait_ge(weights_loaded, 16 * (n + 1))
                with pool.Fori(0, LOAD // CHECK) as i:
                    at = i * 3 + (n * (LOAD // CHECK) * 3 + 2)
                    pool.wait_ge(low_step, at)
                    pool.tensor_tensor(low[:], weights[:, bass.ds(i * CHECK + n * LOAD, CHECK)].bitcast(U32),
                                       low_shift[:].to_broadcast([P, CHECK]), ALU.mult).then_inc(low_step, 1)
                    pool.wait_ge(low_step, at + 1)
                    pool.tensor_tensor(low[:], low[:], low_shift[:].to_broadcast([P, CHECK]), ALU.divide)\
                        .then_inc(low_step, 1)
                    pool.wait_ge(low_step, at + 2)
                    pool.tensor_tensor(low_sum[:], low_sum[:], low[:], ALU.add).then_inc(low_step, 1)

        @block.scalar
        def _(act):
            act.preload_act_table_set("natural_log_exp_and_others")
            for i, scale in enumerate((float(D) ** -0.5, 1.0)):
                act.wait_ge(misc_full, i + 1)
                act.activation(proj[:, i, 0].rearrange("p k n -> p (k n)"), ps[:, MISC_BANKS[i]], ACT.Copy,
                               scale=scale).then_inc(misc_hi, 1)

            with act.Fori(0, B) as b:
                def hi_of(use, dst):
                    act.wait_ge(misc_full, misc_count(b, use))
                    n = dst.shape[-1]
                    act.copy(dst, ps[:, misc_bank(use), 0:n]).then_inc(misc_hi, 1)

                def ln_rstd(g):
                    act.wait_ge(moments_done, b * GROUPS + g + 1)
                    act.activation(log_var[:], d_var[:], ACT.Ln, scale=1.0 / D, bias=LN_EPS).then_inc(log_done, 1)
                    act.wait_ge(log_done, b * GROUPS + g + 1)
                    act.activation(rstd0[:], log_var[:], ACT.Exp, scale=-0.5).then_inc(rstd0_done, 1)

                def hi_xT(g):
                    for k in range(KD):
                        hi_of(("xT", g, k), xnT[:, g, 0, k])

                def hi_proj(g):
                    for m in range(KD):
                        hi_of(("y", g, m), yT[:, 0, m])
                    for h in range(2):
                        use = ("v", g, h)
                        act.wait_ge(misc_full, misc_count(b, use))
                        act.copy(val[:, g * PER + 2 * h:g * PER + 2 * h + 2, 0],
                                 ps[:, misc_bank(use)].rearrange("p (t n) -> p t n", t=2)).then_inc(misc_hi, 1)

                def hi_pT(t, c):
                    n = piece(t, c)
                    if n >= PT_SLOTS:
                        act.wait_ge(out_full, b * PIECES + n - PT_SLOTS + 1)
                    hi_of(("pT", t, c), probsT[:, n % PT_SLOTS, 0, 0:width(t, c)])

                def exp(t):
                    act.wait_ge(max_ready, b * TILES + t + 1)
                    for c in range(pieces(t)):
                        if t and c < pieces(t - 1):
                            act.wait_ge(misc_full, misc_count(b, ("pT", t - 1, c)))
                        n = width(t, c)
                        act.activation(probs[:, c * BANK:c * BANK + n], ps[:, c, 0:n], ACT.Exp,
                                       bias=neg_max[:, t % 2:t % 2 + 1],
                                       accum_out=piece_sum[:, t % 2, c:c + 1]).then_inc(probs_ready, 1)

                ln_rstd(0)
                hi_xT(0)
                hi_proj(0)
                exp(0)
                for t in range(TILES):
                    g = t // PER + 1
                    for c in range(min(2, pieces(t))):
                        hi_pT(t, c)
                    if g < GROUPS and t % PER == 1:
                        ln_rstd(g)
                    if g < GROUPS and t % PER == 2:
                        hi_xT(g)
                    if g < GROUPS and t % PER == 3:
                        hi_proj(g)
                    for c in range(2, pieces(t)):
                        hi_pT(t, c)
                    if t + 1 < TILES:
                        exp(t + 1)
                act.wait_ge(xn_stored, b * (16 * GROUPS) + 16 * GROUPS)

            act.wait_ge(scores_full, B * PIECES)
            for u in range(2):
                act.dma_start(chunk_x[:, u].rearrange("p l k n -> p (l k n)").bitcast(F32),
                              xn_dram[u * P:(u + 1) * P, :]).then_inc(chunk_loaded[u], 16)
            act.wait_ge(scales_loaded, 80)
            with act.Fori(0, CHUNKS // 2) as it:
                for u in range(2):
                    c = it * 2 + u
                    for n in range(3 * KH):
                        if n >= 4:
                            act.wait_ge(hid_ready, c * (3 * KH) + n - 3)
                        layer, j = divmod(n, KH)
                        if layer == 0:
                            act.wait_ge(pre_full, c * 32 + 2 * j + 1)
                            act.activation(act_out[:, n % 4], ps[:, 2 * (j % 2)], ACT.Silu,
                                           scale=scale_in[:, 0, j:j + 1]).then_inc(act_done, 1)
                        else:
                            act.wait_ge(pre_full, c * 32 + (2 + layer - 1) * KH + j + 1)
                            act.activation(act_out[:, n % 4], ps[:, j % 4], ACT.Gelu,
                                           scale=scale_hid[:, layer - 1, j:j + 1]).then_inc(act_done, 1)

        @block.vector
        def _(dve):
            def lo(dst, whole, hi, done):
                return dve.tensor_tensor(dst, whole, hi.bitcast(F32), ALU.subtract).then_inc(done, 1)

            for i, scale in enumerate((float(D) ** -0.5, 1.0)):
                dve.wait_ge(misc_hi, i + 1)
                dve.scalar_tensor_tensor(
                    out=proj[:, i, 1].rearrange("p k n -> p (k n)"), in0=ps[:, MISC_BANKS[i]], scalar=scale,
                    in1=proj[:, i, 0].rearrange("p k n -> p (k n)").bitcast(F32), op0=ALU.mult, op1=ALU.subtract
                ).then_inc(misc_empty, 1)
            dve.memset(row_sum[:], 1.0).then_inc(out_evacuated, 1)

            with dve.Fori(0, B) as b:
                def ln_moments(g):
                    dve.wait_ge(x_loaded, b * (16 * GROUPS) + 16 * (g + 1))
                    for r in range(PER):
                        last = dve.bn_stats(stats[:, r], xs[:, r])
                    last.then_inc(stats_done, 1)
                    at = b * (2 * GROUPS) + 2 * g
                    dve.wait_ge(stats_done, b * GROUPS + g + 1)
                    dve.tensor_tensor(halves[:, 0], stats[:, :, 1], stats[:, :, 4], ALU.add)
                    dve.tensor_tensor(halves[:, 1], stats[:, :, 1], stats[:, :, 4], ALU.subtract)
                    dve.tensor_tensor(halves[:, 2], stats[:, :, 2], stats[:, :, 5], ALU.add).then_inc(moment_step, 1)
                    dve.wait_ge(moment_step, at + 1)
                    dve.tensor_scalar(mean[:], halves[:, 0], 0.5, None, ALU.mult)
                    dve.tensor_tensor(halves[:, 3], halves[:, 1], halves[:, 1], ALU.mult).then_inc(moment_step, 1)
                    dve.wait_ge(moment_step, at + 2)
                    dve.scalar_tensor_tensor(out=d_var[:], in0=halves[:, 3], scalar=D / 4, in1=halves[:, 2],
                                             op0=ALU.mult, op1=ALU.add).then_inc(moments_done, 1)

                def ln_apply(g):
                    at = b * (3 * GROUPS) + 3 * g
                    dve.wait_ge(rstd0_done, b * GROUPS + g + 1)
                    dve.tensor_tensor(newton[:, 0], rstd0[:], rstd0[:], ALU.mult)
                    dve.tensor_scalar(newton[:, 1], d_var[:], 1.0 / D, LN_EPS, ALU.mult, ALU.add)\
                       .then_inc(newton_step, 1)
                    dve.wait_ge(newton_step, at + 1)
                    dve.scalar_tensor_tensor(out=newton[:, 2], in0=newton[:, 0], scalar=-0.5, in1=newton[:, 1],
                                             op0=ALU.mult, op1=ALU.mult).then_inc(newton_step, 1)
                    dve.wait_ge(newton_step, at + 2)
                    dve.scalar_tensor_tensor(out=rstd[:], in0=newton[:, 2], scalar=1.5, in1=rstd0[:],
                                             op0=ALU.add, op1=ALU.mult).then_inc(newton_step, 1)
                    dve.wait_ge(newton_step, at + 3)
                    for r in range(PER):
                        last = dve.tensor_scalar(xs[:, r], xs[:, r], mean[:, r:r + 1], rstd[:, r:r + 1],
                                                 ALU.subtract, ALU.mult)
                    last.then_inc(xn_ready, 1)

                def lo_of(use, hi, dst):
                    dve.wait_ge(misc_hi, misc_count(b, use))
                    lo(dst, ps[:, misc_bank(use), 0:dst.shape[-1]], hi, misc_empty)

                def lo_xT(g):
                    for k in range(KD):
                        lo_of(("xT", g, k), xnT[:, g, 0, k], xnT[:, g, 1, k])

                def lo_proj(g):
                    for m in range(KD):
                        lo_of(("y", g, m), yT[:, 0, m], yT[:, 1, m])
                    for h in range(2):
                        use = ("v", g, h)
                        two = slice(g * PER + 2 * h, g * PER + 2 * h + 2)
                        dve.wait_ge(misc_hi, misc_count(b, use))
                        lo(val[:, two, 1], ps[:, misc_bank(use)].rearrange("p (t n) -> p t n", t=2),
                           val[:, two, 0], misc_empty)

                def lo_pT(t, c):
                    slot, n = piece(t, c) % PT_SLOTS, width(t, c)
                    lo_of(("pT", t, c), probsT[:, slot, 0, 0:n], probsT[:, slot, 1, 0:n])

                def row_max(t):
                    n = pieces(t)
                    for c in range(n):
                        dve.wait_ge(scores_full, b * PIECES + piece(t, c) + 1)
                        scores = ps[:, c, 0:width(t, c)]
                        if n == 1:
                            dve.tensor_reduce(neg_max[:, t % 2:t % 2 + 1], scores, X, ALU.max, negate=True)\
                               .then_inc(max_ready, 1)
                        else:
                            dve.tensor_reduce(piece_max[:, c:c + 1], scores, X, ALU.max)\
                               .then_inc(pieces_max_done, 1)
                    if n > 1:
                        dve.wait_ge(pieces_max_done, b * (PIECES - PER) + piece(t) - PER + n)
                        dve.tensor_reduce(neg_max[:, t % 2:t % 2 + 1], piece_max[:, 0:n], X, ALU.max, negate=True)\
                           .then_inc(max_ready, 1)

                def finish(t):
                    n = pieces(t)
                    at = b * (2 * TILES) + 2 * t
                    dve.wait_ge(probs_ready, b * PIECES + piece(t, n))
                    dve.tensor_reduce(row_sum[:], piece_sum[:, t % 2, 0:n], X, ALU.add).then_inc(norm_step, 1)
                    dve.wait_ge(norm_step, at + 1)
                    dve.reciprocal(row_inv[:], row_sum[:]).then_inc(norm_step, 1)
                    dve.wait_ge(norm_step, at + 2)
                    slot = t % RES_SLOTS
                    dve.wait_ge(res_loaded[slot], b * (16 * PER) + 16 * (t // RES_SLOTS + 1))
                    dve.wait_ge(out_full, b * PIECES + piece(t, n))
                    dve.scalar_tensor_tensor(out=res[:, slot], in0=ps[:, OUT_BANK, 0:D], scalar=row_inv[:],
                                             in1=res[:, slot], op0=ALU.mult, op1=ALU.add).then_inc(out_evacuated, 1)

                ln_moments(0)
                ln_apply(0)
                lo_xT(0)
                lo_proj(0)
                row_max(0)
                for t in range(TILES):
                    g = t // PER + 1
                    for c in range(min(2, pieces(t))):
                        lo_pT(t, c)
                    if g < GROUPS and t % PER == 2:
                        lo_xT(g)
                    if g < GROUPS and t % PER == 3:
                        lo_proj(g)
                    if t + 1 < TILES:
                        row_max(t + 1)
                    for c in range(2, pieces(t)):
                        lo_pT(t, c)
                    if g < GROUPS and t % PER == 0:
                        ln_moments(g)
                    if g < GROUPS and t % PER == 1:
                        ln_apply(g)
                    finish(t)

            dve.wait_ge(low_step, 2 + 3 * (WCOLS // CHECK))
            dve.tensor_reduce(low_any[:], low_sum[:], X, ALU.max).then_inc(low_ready, 1)
            dve.wait_ge(low_summed, 1)
            dve.tensor_scalar(inexact[:], ps[0:1, MISC_BANKS[0], 0:1], 0.0, None, ALU.is_gt).then_inc(inexact_ready, 1)

            dve.wait_ge(scales_loaded, 80)
            with dve.Fori(0, CHUNKS // 2) as it:
                for u in range(2):
                    c = it * 2 + u
                    for n in range(3 * KH):
                        layer, j = divmod(n, KH)
                        dst = hidden[(u + layer) % 2][:, j]
                        whole = act_out[:, n % 4]
                        dve.wait_ge(act_done, c * (3 * KH) + n + 1)
                        if layer == 0:
                            dve.wait_ge(pre_full, c * 32 + 2 * j + 2)
                            dve.scalar_tensor_tensor(out=gated[:, j % 2], in0=ps[:, 2 * (j % 2) + 1],
                                                     scalar=scale_in[:, 1, j:j + 1], in1=whole,
                                                     op0=ALU.mult, op1=ALU.mult).then_inc(gate_done, 1)
                            whole = gated[:, j % 2]
                            dve.wait_ge(gate_done, c * KH + j + 1)
                        dve.tensor_copy(dst[:, 0], whole).then_inc(hi_done, 1)
                        dve.wait_ge(hi_done, c * (3 * KH) + n + 1)
                        lo(dst[:, 1], whole, dst[:, 0], hid_ready)
                    dve.wait_ge(res_chunk_loaded, c * 16 + 16)
                    for r in range(PER):
                        dve.wait_ge(ffn_full, c * PER + r + 1)
                        dve.tensor_tensor(gated[:, r % 2, 0:D], ps[:, 4 + r, 0:D], scale_out[:], ALU.mult)\
                           .then_inc(ffn_scaled, 1)
                        dve.wait_ge(ffn_scaled, c * PER + r + 1)
                        dve.tensor_tensor(res[:, r], res[:, r], gated[:, r % 2, 0:D], ALU.add)\
                           .then_inc(out_evacuated, 1)

        @block.tensor
        def _(pe):
            pe.wait_ge(attn_w_loaded, 64)
            for i, (lhs, rhs) in enumerate(((0, 1), (2, 3))):
                for m in range(KD):
                    for k in range(KD):
                        mm = pe.matmul(ps[:, MISC_BANKS[i], m * D:(m + 1) * D], attn_w[:, lhs, k, m * P:(m + 1) * P],
                                       attn_w[:, rhs, k], start=(k == 0), stop=(k == KD - 1))
                mm.then_inc(misc_full, 1)
            pe.wait_ge(consts_ready, 4)

            PARTS = ((0, 0), (0, 1), (1, 0))

            def split_product(dst, lhs, rhs, start=True, stop=True):
                for k in range(KD):
                    for n, (p, q) in enumerate(PARTS):
                        mm = pe.matmul(dst, lhs(p, k), rhs(q, k), start=start and k == 0 and n == 0,
                                       stop=stop and k == KD - 1 and n == len(PARTS) - 1)
                return mm

            with pe.Fori(0, B) as b:
                def take_bank(use):
                    n = MISC[use]
                    pe.wait_ge(misc_empty, b * len(MISC) + MISC0 + max(0, n - len(MISC_BANKS) + 1))
                    return ps[:, misc_bank(use)]

                def transpose_x(g):
                    pe.wait_ge(xn_ready, b * GROUPS + g + 1)
                    for k in range(KD):
                        bank = take_bank(("xT", g, k))
                        for r in range(PER):
                            mm = pe.transpose(bank[:, r * P:(r + 1) * P], xs[:, r, k * P:(k + 1) * P], ident[:])
                        mm.then_inc(misc_full, 1)

                def project(g):
                    pe.wait_ge(misc_empty, misc_count(b, ("xT", g, KD - 1)))
                    for m in range(KD):
                        split_product(take_bank(("y", g, m)), lambda p, k: proj[:, 0, p, k, m * P:(m + 1) * P],
                                      lambda q, k: xnT[:, g, q, k]).then_inc(misc_full, 1)
                    for h in range(2):
                        bank = take_bank(("v", g, h))
                        for i in range(2):
                            r = 2 * h + i
                            mm = split_product(bank[:, i * D:(i + 1) * D],
                                               lambda p, k: xnT[:, g, p, k, r * P:(r + 1) * P],
                                               lambda q, k: proj[:, 1, q, k])
                        mm.then_inc(misc_full, 1)

                def score(t):
                    g, r = divmod(t, PER)
                    if r == 0:
                        pe.wait_ge(misc_empty, misc_count(b, ("y", g, KD - 1)))
                    for c in range(pieces(t)):
                        if t and c < pieces(t - 1):
                            pe.wait_ge(probs_ready, b * PIECES + piece(t - 1, c) + 1)
                        n = width(t, c)
                        mm = split_product(ps[:, c, 0:n], lambda p, k: yT[:, p, k, r * P:(r + 1) * P],
                                           lambda q, k: xnT[:, c, q, k, 0:n], stop=c < g)
                        if c == g:
                            mm = pe.matmul(ps[:, c, r * P:(r + 1) * P], ident_h[:], mask[:], start=False, stop=True)
                        mm.then_inc(scores_full, 1)

                def transpose_probs(t, c):
                    pe.wait_ge(probs_ready, b * PIECES + piece(t, c) + 1)
                    bank = take_bank(("pT", t, c))
                    for i in range(width(t, c) // P):
                        mm = pe.transpose(bank[:, i * P:(i + 1) * P],
                                          probs[:, c * BANK + i * P:c * BANK + (i + 1) * P], ident[:])
                    mm.then_inc(misc_full, 1)

                def attend(t, c):
                    if c == 0:
                        pe.wait_ge(out_evacuated, b * TILES + t + 1)
                    pe.wait_ge(misc_empty, misc_count(b, ("pT", t, c)))
                    slot, n = piece(t, c) % PT_SLOTS, width(t, c) // P
                    for i in range(n):
                        for j, (p, q) in enumerate(PARTS):
                            mm = pe.matmul(ps[:, OUT_BANK, 0:D], probsT[:, slot, p, i * P:(i + 1) * P],
                                           val[:, c * PER + i, q], start=(c == 0 and i == 0 and j == 0),
                                           stop=(c == pieces(t) - 1 and i == n - 1 and j == len(PARTS) - 1))
                    mm.then_inc(out_full, 1)

                transpose_x(0)
                project(0)
                score(0)
                for t in range(TILES):
                    g, n = t // PER + 1, pieces(t)
                    for c in range(min(2, n)):
                        transpose_probs(t, c)
                    if g < GROUPS and t % PER == 2:
                        transpose_x(g)
                    if g < GROUPS and t % PER == 3:
                        project(g)
                    if t + 1 < TILES:
                        score(t + 1)
                    for c in range(n):
                        if c + 2 < n:
                            transpose_probs(t, c + 2)
                        attend(t, c)

            pe.wait_ge(low_ready, 1)
            pe.matmul(ps[0:1, MISC_BANKS[0], 0:1], low_any[:], ones[:], start=True, stop=True).then_inc(low_summed, 1)
            pe.wait_ge(inexact_ready, 1)
            some_low = pe.value_load(inexact[0:1, 0:1])

            def feed_forward(view):
                def layer_tile(dst, at, j, src, ks, ready=None):
                    for k in range(ks):
                        if ready is not None:
                            pe.wait_ge(hid_ready, ready + k + 1)
                        for p in range(2):
                            mm = pe.matmul(dst, view(weights[:, at + k * HID + j * P:at + k * HID + (j + 1) * P]),
                                           view(src(p, k)), start=(k == 0 and p == 0),
                                           stop=(k == ks - 1 and p == 1))
                    mm.then_inc(pre_full, 1)

                with pe.Fori(0, CHUNKS // 2) as it:
                    for u in range(2):
                        c = it * 2 + u
                        pe.wait_ge(chunk_loaded[u], it * 16 + 16)
                        for j in range(KH):
                            if j >= 2:
                                pe.wait_ge(gate_done, c * KH + j - 1)
                            for i, at in enumerate((W1, W2)):
                                layer_tile(ps[:, 2 * (j % 2) + i], at, j, lambda p, k: chunk_x[:, u, p, k], KD)
                        for layer, at in ((1, H1), (2, H2)):
                            src = hidden[(u + layer + 1) % 2]
                            for j in range(KH):
                                if layer == 1 and j < 4:
                                    pe.wait_ge(gate_done, c * KH + KH - 1 + j // 2)
                                else:
                                    pe.wait_ge(act_done, c * (3 * KH) + layer * KH + j - 3)
                                layer_tile(ps[:, j % 4], at, j, lambda p, k: src[:, k, p], KH,
                                           c * (3 * KH) + (layer - 1) * KH if j == 0 else None)
                        src = hidden[u]
                        pe.wait_ge(out_evacuated, c * PER + (B * TILES + 1))
                        for k in range(KH):
                            pe.wait_ge(hid_ready, c * (3 * KH) + 2 * KH + k + 1)
                            for r in range(PER):
                                for p in range(2):
                                    mm = pe.matmul(ps[:, 4 + r, 0:D], view(src[:, k, p, r * P:(r + 1) * P]),
                                                   view(weights[:, W3 + k * D:W3 + (k + 1) * D]),
                                                   start=(k == 0 and p == 0), stop=(k == KH - 1 and p == 1))
                                if k == KH - 1:
                                    mm.then_inc(ffn_full, 1)

            with pe.If(some_low == 0):
                feed_forward(lambda a: a)
            with pe.Else():
                feed_forward(lambda a: a.bitcast(F32))


_FFN_W = ("L0_ffn_w1_w", "L0_ffn_w2_w", "L0_ffn_h1_w", "L0_ffn_h2_w", "L0_ffn_w3_w")
_SCALES = ("L0_ffn_w1_s", "L0_ffn_w2_s", "L0_ffn_h1_s", "L0_ffn_h2_s")


def kernel(**inputs):
    import numpy as np
    import concourse.bacc as bacc
    from concourse.bass_utils import run_bass_kernel_spmd

    arrays = {"x": np.asarray(inputs["L0_attn_x"])}
    for name in ("Wq", "Wk", "Wv"):
        arrays[name + "T"] = np.asarray(inputs["L0_attn_" + name]).T
    arrays["Wo"] = np.asarray(inputs["L0_attn_Wo"])
    tiles = [np.asarray(inputs[n]).T.reshape(-1, P, inputs[n].shape[0]).transpose(1, 0, 2).reshape(P, -1) for n in _FFN_W]
    arrays["ffn_w"] = np.concatenate(tiles, axis=1).reshape(P, LOADS, LOAD).transpose(1, 0, 2)
    for name in _SCALES:
        arrays[name] = np.asarray(inputs[name]).reshape(KH, P).T
    arrays["w3_s"] = np.asarray(inputs["L0_ffn_w3_s"])

    nc = bacc.Bacc("TRN2", target_bir_lowering=False, num_devices=1)
    arrays = {"in_" + n: np.ascontiguousarray(a) for n, a in arrays.items()}
    args = [nc.dram_tensor(n, a.shape, mybir.dt.from_np(a.dtype), kind="ExternalInput").ap() for n, a in arrays.items()]
    out = nc.dram_tensor("out_0", (B, S, D), F32, kind="ExternalOutput").ap()
    build(nc, *args, out)
    r = run_bass_kernel_spmd(nc, [arrays], core_ids=[0])
    return r.results[0]["out_0"]
```

```python
from contextlib import ExitStack

import concourse.bass as bass
from concourse import mybir

F32 = mybir.dt.float32
F32R = mybir.dt.float32r
BF16 = mybir.dt.bfloat16
I32 = mybir.dt.int32
U32 = mybir.dt.uint32
ALU = mybir.AluOpType
ACT = mybir.ActivationFunctionType
X = mybir.AxisListType.X

P = 128
BANK = 512
B, S, D = 2, 2048, 256
HID = 1024
KD = D // P
KH = HID // P
GROUP = BANK
GROUPS = S // GROUP
TILES = S // P
PER = GROUP // P
CHUNKS = B * GROUPS
LN_EPS = 1e-5
MASKED = -3.0e38
LOW_BITS = 12

MISC_BANKS = (4, 5, 6)
OUT_BANK = 7
PT_SLOTS = 4
RES_SLOTS = 4

W1, W2, H1, H2, W3 = 0, KD * HID, 2 * KD * HID, 2 * KD * HID + KH * HID, 2 * KD * HID + 2 * KH * HID
WCOLS = W3 + KH * D
LOAD = 2048
LOADS = WCOLS // LOAD
WARM_UP = 32
CHECK = 512


def pieces(t):
    return t // PER + 1


def width(t, c):
    return BANK if c < t // PER else (t % PER + 1) * P


def piece(t, c=0):
    return sum(pieces(i) for i in range(t)) + c


PIECES = piece(TILES)
AHEAD = 3


def scores_at(t, c):
    return t if t < PER else c


def last_at(t, c):
    if t < PER:
        return None
    return (t - 1, c) if t > PER and c < pieces(t - 1) else (c, 0)


def scored(t):
    if t < PER - 1:
        return [t + AHEAD] if t + AHEAD < PER else []
    return [t + 1] if t + 1 < TILES else []


def transposed(t):
    if t < PER:
        return [(i, 0) for i in range(t + (t > 0), min(t + 2, PER))]
    return [(t, c) for c in range(min(2, pieces(t)))]


def misc_order():
    order = [("xT", 0, 0), ("xT", 0, 1), ("y", 0, 0), ("y", 0, 1), ("v", 0, 0), ("v", 0, 1)]
    for t in range(TILES):
        g = t // PER + 1
        order += [("pT", i, c) for i, c in transposed(t)]
        if g < GROUPS and t % PER == 2:
            order += [("xT", g, 0), ("xT", g, 1)]
        if g < GROUPS and t % PER == 3:
            order += [("y", g, 0), ("y", g, 1), ("v", g, 0), ("v", g, 1)]
        order += [("pT", t, c) for c in range(2, pieces(t))]
    return {use: n for n, use in enumerate(order)}


MISC = misc_order()
SIDE_USE = ("v", 0, 1)
RING = [use for use in MISC if use != SIDE_USE]
assert len(RING) % len(MISC_BANKS) == 0
A_BANK = MISC_BANKS[RING.index(("y", 0, 0)) % len(MISC_BANKS)]


def misc_bank(use):
    return OUT_BANK if use == SIDE_USE else MISC_BANKS[RING.index(use) % len(MISC_BANKS)]


def misc_count(b, use, ahead=0):
    return b * len(MISC) + (ahead * len(MISC) + MISC[use] + 1)


def build(nc, x, wqT, wkT, wvT, wo, ffn_w, s1, s2, sh1, sh2, s3, out):
    xf = x.rearrange("b s d -> (b s) d")
    outf = out.rearrange("b s d -> (b s) d")
    raw_w = nc.dram_tensor("raw_w", [LOADS, P, LOAD], F32, kind="Internal").ap()
    xn_dram = nc.dram_tensor("xn_dram", [CHUNKS * P, 2 * KD * GROUP], F32, kind="Internal").ap()
    res_dram = nc.dram_tensor("res_dram", [B * S, D], F32, kind="Internal").ap()

    with ExitStack() as ctx:
        def sb(name, shape, dt):
            return ctx.enter_context(nc.sbuf_tensor(name, shape, dt))

        def sem(name):
            return ctx.enter_context(nc.semaphore(name))

        weights = sb("weights", [P, WCOLS], F32R)
        XT, VV, YT, PT = 0, 2 * KD * S, 2 * KD * S + 2 * TILES * D, 2 * KD * S + 2 * TILES * D + 2 * KD * GROUP
        REGION = PT + PT_SLOTS * 2 * BANK
        region = sb("region", [P, REGION], F32R)
        xnT = region[:, XT:VV].rearrange("p (g l k n) -> p g l k n", g=GROUPS, l=2, k=KD)
        val = region[:, VV:YT].rearrange("p (t l n) -> p t l n", t=TILES, l=2)
        yT = region[:, YT:PT].rearrange("p (l k n) -> p l k n", l=2, k=KD)
        probsT = region[:, PT:REGION].rearrange("p (s l n) -> p s l n", s=PT_SLOTS, l=2)
        CHUNK_COLS, HID_COLS = 2 * KD * GROUP, 2 * KH * GROUP
        chunk_x = region[:, 0:2 * CHUNK_COLS].rearrange("p (u l k n) -> p u l k n", u=2, l=2, k=KD)
        hidden = [region[:, 2 * CHUNK_COLS + i * HID_COLS:2 * CHUNK_COLS + (i + 1) * HID_COLS]
                  .rearrange("p (k l n) -> p k l n", k=KH, l=2) for i in range(2)]
        proj = sb("proj", [P, 2, 2, KD, D], F32R)
        probs = sb("probs", [P, S], F32)
        attn_w = probs[:, :].rearrange("p (w k n) -> p w k n", w=4, k=KD)
        act_out = probs[:, :].rearrange("p (u n) -> p u n", u=4)
        xs = sb("xs", [P, PER, D], F32)
        gated = xs[:, :, :].rearrange("p r n -> p (r n)").rearrange("p (u n) -> p u n", u=2)
        res = sb("res", [P, RES_SLOTS, D], F32)
        ident = sb("ident", [P, P], F32)
        ident_h = sb("ident_h", [P, P], BF16)
        mask = sb("mask", [P, P], BF16)
        low = sb("low", [P, CHECK], U32)
        low_shift = sb("low_shift", [P, 1], U32)
        low_sum = sb("low_sum", [P, CHECK], U32)
        low_any = sb("low_any", [P, 1], F32)
        ones = sb("ones", [P, 1], F32)
        inexact = sb("inexact", [1, 1], I32)
        scale_in = sb("scale_in", [P, 2, KH], F32)
        scale_hid = sb("scale_hid", [P, 2, KH], F32)
        scale_out = sb("scale_out", [P, D], F32)
        stats = sb("stats", [P, PER, 6], F32)
        halves = sb("halves", [P, 4, PER], F32)
        mean = sb("mean", [P, PER], F32)
        d_var = sb("d_var", [P, PER], F32)
        log_var = sb("log_var", [P, PER], F32)
        newton = sb("newton", [P, 3, PER], F32)
        rstd0 = sb("rstd0", [P, PER], F32)
        rstd = sb("rstd", [P, PER], F32)
        piece_max = sb("piece_max", [P, 4], F32)
        neg_max = sb("neg_max", [P, PER], F32)
        piece_sum = sb("piece_sum", [P, PER, 4], F32)
        row_sum = sb("row_sum", [P, 1], F32)
        row_inv = sb("row_inv", [P, 1], F32)

        ps = ctx.enter_context(nc.psum_tensor("ps", [P, 8, BANK], F32))

        qk_loaded = sem("qk_loaded")
        vo_loaded = sem("vo_loaded")
        consts_ready = sem("consts_ready")
        pool_fill = sem("pool_fill")
        scales_loaded = sem("scales_loaded")
        raw_copied = sem("raw_copied")
        weights_loaded = sem("weights_loaded")
        x_loaded = sem("x_loaded")
        stats_done = sem("stats_done")
        moment_step = sem("moment_step")
        moments_done = sem("moments_done")
        log_done = sem("log_done")
        rstd0_done = sem("rstd0_done")
        newton_step = sem("newton_step")
        xn_ready = sem("xn_ready")
        proj_full = sem("proj_full")
        proj_hi = sem("proj_hi")
        proj_ready = sem("proj_ready")
        misc_full = sem("misc_full")
        misc_hi = sem("misc_hi")
        misc_empty = sem("misc_empty")
        scores_full = sem("scores_full")
        pieces_max_done = sem("pieces_max_done")
        max_ready = sem("max_ready")
        probs_ready = sem("probs_ready")
        out_full = sem("out_full")
        norm_step = sem("norm_step")
        out_evacuated = sem("out_evacuated")
        res_loaded = [sem(f"res_loaded{i}") for i in range(RES_SLOTS)]
        res_stored = [sem(f"res_stored{i}") for i in range(RES_SLOTS)]
        xn_stored = sem("xn_stored")
        low_step = sem("low_step")
        low_ready = sem("low_ready")
        low_summed = sem("low_summed")
        inexact_ready = sem("inexact_ready")
        chunk_loaded = [sem(f"chunk_loaded{i}") for i in range(2)]
        res_chunk_loaded = sem("res_chunk_loaded")
        pre_full = sem("pre_full")
        act_done = sem("act_done")
        gate_done = sem("gate_done")
        hi_done = sem("hi_done")
        hid_ready = sem("hid_ready")
        ffn_full = sem("ffn_full")
        ffn_scaled = sem("ffn_scaled")
        out_stored = sem("out_stored")

        block = ctx.enter_context(nc.Block())

        def rows(first, n):
            return bass.ds(first, n)

        def in_range(first, most):
            return nc.s_assert_within(first, 0, most, skip_runtime_bounds_check_because="the branch leaves out the last")

        def group_rows(dram, first):
            return dram[rows(first, GROUP), :].rearrange("(r p) d -> p r d", p=P)

        @block.sync
        def _(sp):
            sp.dma_start(xs[:], group_rows(xf, 0)).then_inc(x_loaded, 16)
            for i, w in enumerate((wqT, wkT, wvT, wo)):
                sp.dma_start(attn_w[:, i], w.rearrange("(k p) n -> p k n", p=P)
                             ).then_inc(qk_loaded if i < 2 else vo_loaded, 16)
            for i, s in enumerate((s1, s2)):
                sp.dma_start(scale_in[:, i], s).then_inc(scales_loaded, 16)
            for i, s in enumerate((sh1, sh2)):
                sp.dma_start(scale_hid[:, i], s).then_inc(scales_loaded, 16)
            sp.dma_start(scale_out[:], s3.partition_broadcast(P)).then_inc(scales_loaded, 16)

            def load_res(first, t):
                sp.dma_start(res[:, t % RES_SLOTS], xf[rows(first + t * P, P), :]).then_inc(res_loaded[t % RES_SLOTS], 16)

            for t in range(RES_SLOTS - 1):
                load_res(0, t)

            def load_x(b, g, first, ahead=0):
                sp.wait_ge(misc_full, misc_count(b, ("xT", g, KD - 1), ahead))
                sp.dma_start(xs[:], group_rows(xf, first)).then_inc(x_loaded, 16)

            load_x(0, 0, GROUP)
            with sp.Fori(0, B) as b:
                def store_xn(g):
                    sp.wait_ge(misc_empty, misc_count(b, ("xT", g, 1)))
                    sp.dma_start(xn_dram[rows(b * (GROUPS * P) + g * P, P), :],
                                 xnT[:, g].rearrange("p l k n -> p (l k n)").bitcast(F32)
                                 ).then_inc(xn_stored, 16)

                for t in range(TILES):
                    g = t // PER
                    if t == TILES - 1:
                        with sp.If(b < B - 1):
                            load_x(b, 0, in_range((b + 1) * S + GROUP, (B - 1) * S + GROUP), 1)
                        with sp.Else():
                            sp.wait_ge(scores_full, B * PIECES)
                            sp.wait_ge(xn_stored, B * (16 * GROUPS))
                            for u in range(2):
                                sp.dma_start(chunk_x[:, u].rearrange("p l k n -> p (l k n)").bitcast(F32),
                                             xn_dram[u * P:(u + 1) * P, :]).then_inc(chunk_loaded[u], 16)
                    if t % PER == 0:
                        store_xn(g)
                    sp.wait_ge(out_evacuated, b * TILES + t + 2)
                    sp.dma_start(res_dram[rows(b * S + t * P, P), :], res[:, t % RES_SLOTS]
                                 ).then_inc(res_stored[t % RES_SLOTS], 16)
                    if t % PER == 2:
                        if g + 2 < GROUPS:
                            load_x(b, g + 1, b * S + (g + 2) * GROUP)
                        elif g + 2 == GROUPS:
                            with sp.If(b < B - 1):
                                load_x(b, g + 1, in_range((b + 1) * S, (B - 1) * S))
                    n = t + RES_SLOTS - 1
                    if n < TILES:
                        if n >= RES_SLOTS:
                            sp.wait_ge(res_stored[n % RES_SLOTS], b * (16 * PER) + 16 * (n // RES_SLOTS))
                        load_res(b * S, n)
                with sp.If(b < B - 1):
                    for t in range(RES_SLOTS - 1):
                        sp.wait_ge(res_stored[t], b * (16 * PER) + 16 * PER)
                        load_res(in_range((b + 1) * S, (B - 1) * S), t)

            def load_res_chunk(first):
                sp.dma_start(res[:], group_rows(res_dram, first)).then_inc(res_chunk_loaded, 16)

            for i in range(RES_SLOTS):
                sp.wait_ge(res_stored[i], B * PER * 16)
            load_res_chunk(0)
            with sp.Fori(0, CHUNKS // 2) as it:
                for u in range(2):
                    c = it * 2 + u
                    with sp.If(it < CHUNKS // 2 - 1):
                        sp.wait_ge(pre_full, c * 32 + 16)
                        sp.dma_start(chunk_x[:, u].rearrange("p l k n -> p (l k n)").bitcast(F32),
                                     xn_dram[rows(in_range(it * (2 * P) + (u + 2) * P, (CHUNKS - 1) * P), P), :]
                                     ).then_inc(chunk_loaded[u], 16)
                    for h in range(2):
                        two = PER // 2
                        sp.wait_ge(out_evacuated, c * PER + (B * TILES + 1 + (h + 1) * two))
                        first = it * (2 * GROUP) + (u * GROUP + h * two * P)
                        sp.dma_start(outf[rows(first, two * P), :].rearrange("(r p) d -> p r d", p=P),
                                     res[:, h * two:(h + 1) * two]).then_inc(out_stored, 16)
                    if u == 0:
                        sp.wait_ge(out_stored, c * 32 + 32)
                        load_res_chunk(it * (2 * GROUP) + GROUP)
                    else:
                        with sp.If(it < CHUNKS // 2 - 1):
                            sp.wait_ge(out_stored, c * 32 + 32)
                            load_res_chunk(in_range((it + 1) * (2 * GROUP), (CHUNKS - 2) * GROUP))
            sp.wait_ge(out_stored, CHUNKS * 32)

        @block.gpsimd
        def _(pool):
            pool.memset(ident[:], 0.0).then_inc(pool_fill, 1)
            pool.memset(ident_h[:], 0.0).then_inc(pool_fill, 1)
            pool.memset(mask[:], 0.0).then_inc(pool_fill, 1)
            pool.memset(ones[:], 1.0).then_inc(consts_ready, 1)
            pool.wait_ge(pool_fill, 3)
            for i in (ident, ident_h):
                pool.affine_select(out=i[:], in_=i[:], pattern=[[-1, P]], compare_op=ALU.not_equal, fill=1.0,
                                   base=0, channel_multiplier=1).then_inc(consts_ready, 1)
            pool.affine_select(out=mask[:], in_=mask[:], pattern=[[-1, P]], compare_op=ALU.is_ge, fill=MASKED,
                               base=0, channel_multiplier=1).then_inc(consts_ready, 1)
            pool.memset(low_shift[:], 1 << (32 - LOW_BITS)).then_inc(low_step, 1)
            pool.memset(low_sum[:], 0).then_inc(low_step, 1)
            pool.wait_ge(x_loaded, 16)
            pool.wait_ge(qk_loaded, 32)
            pool.wait_ge(vo_loaded, 32)
            pool.dma_start(raw_w[0], ffn_w[0]).then_inc(raw_copied, 16)
            for n in range(LOADS):
                pool.wait_ge(raw_copied, 16 * (n + 1))
                pool.dma_start(weights[:, n * LOAD:(n + 1) * LOAD].bitcast(F32), raw_w[n]).then_inc(weights_loaded, 16)
                if n + 1 < LOADS:
                    pool.dma_start(raw_w[n + 1], ffn_w[n + 1]).then_inc(raw_copied, 16)
                pool.wait_ge(weights_loaded, 16 * (n + 1))
                with pool.Fori(0, LOAD // CHECK) as i:
                    at = i * 3 + (n * (LOAD // CHECK) * 3 + 2)
                    pool.wait_ge(low_step, at)
                    pool.tensor_tensor(low[:], weights[:, bass.ds(i * CHECK + n * LOAD, CHECK)].bitcast(U32),
                                       low_shift[:].to_broadcast([P, CHECK]), ALU.mult).then_inc(low_step, 1)
                    pool.wait_ge(low_step, at + 1)
                    pool.tensor_tensor(low[:], low[:], low_shift[:].to_broadcast([P, CHECK]), ALU.divide)\
                        .then_inc(low_step, 1)
                    pool.wait_ge(low_step, at + 2)
                    pool.tensor_tensor(low_sum[:], low_sum[:], low[:], ALU.add).then_inc(low_step, 1)

        @block.scalar
        def _(act):
            act.preload_act_table_set("natural_log_exp_and_others")

            def hi_of(b, use, dst, ahead=0):
                act.wait_ge(misc_full, misc_count(b, use, ahead))
                n = dst.shape[-1]
                act.copy(dst, ps[:, misc_bank(use), 0:n]).then_inc(misc_hi, 1)

            def hi_weights(i, bank, scale):
                act.wait_ge(proj_full, i + 1)
                act.activation(proj[:, i, 0].rearrange("p k n -> p (k n)"), ps[:, bank], ACT.Copy,
                               scale=scale).then_inc(proj_hi, 1)

            def ln_rstd(b, g):
                act.wait_ge(moments_done, b * GROUPS + g + 1)
                act.activation(log_var[:], d_var[:], ACT.Ln, scale=1.0 / D, bias=LN_EPS).then_inc(log_done, 1)
                act.wait_ge(log_done, b * GROUPS + g + 1)
                act.activation(rstd0[:], log_var[:], ACT.Exp, scale=-0.5).then_inc(rstd0_done, 1)

            def hi_xT(b, g, ahead=0):
                for k in range(KD):
                    hi_of(b, ("xT", g, k), xnT[:, g, 0, k], ahead)

            def hi_y(b, g, ahead=0):
                for m in range(KD):
                    hi_of(b, ("y", g, m), yT[:, 0, m], ahead)

            def hi_v(b, g, ahead=0):
                for h in range(2):
                    use = ("v", g, h)
                    act.wait_ge(misc_full, misc_count(b, use, ahead))
                    act.copy(val[:, g * PER + 2 * h:g * PER + 2 * h + 2, 0],
                             ps[:, misc_bank(use)].rearrange("p (t n) -> p t n", t=2)).then_inc(misc_hi, 1)

            def hi_pT(b, t, c):
                n = piece(t, c)
                if n >= PT_SLOTS:
                    act.wait_ge(out_full, b * PIECES + n - PT_SLOTS + 1)
                hi_of(b, ("pT", t, c), probsT[:, n % PT_SLOTS, 0, 0:width(t, c)])

            def exp(b, t, ahead=0):
                act.wait_ge(max_ready, b * TILES + (ahead * TILES + t + 1))
                for c in range(pieces(t)):
                    if last_at(t, c):
                        act.wait_ge(misc_full, misc_count(b, ("pT",) + last_at(t, c)))
                    n, r, at = width(t, c), t % PER, scores_at(t, c)
                    act.activation(probs[:, at * BANK:at * BANK + n], ps[:, at, 0:n], ACT.Exp,
                                   bias=neg_max[:, r:r + 1], accum_out=piece_sum[:, r, c:c + 1]
                                   ).then_inc(probs_ready, 1)

            ln_rstd(0, 0)
            hi_weights(0, A_BANK, float(D) ** -0.5)
            hi_xT(0, 0)
            hi_weights(1, OUT_BANK, 1.0)
            hi_y(0, 0)
            for t in range(AHEAD):
                exp(0, t)
            ln_rstd(0, 1)
            hi_v(0, 0)
            with act.Fori(0, B) as b:
                for t in range(TILES):
                    g = t // PER + 1
                    for i, c in transposed(t):
                        hi_pT(b, i, c)
                    if t % PER == 1 and 1 < g < GROUPS:
                        ln_rstd(b, g)
                    if t % PER == 1 and g == GROUPS:
                        with act.If(b < B - 1):
                            ln_rstd(b, GROUPS)
                    if g < GROUPS and t % PER == 2:
                        hi_xT(b, g)
                    if g < GROUPS and t % PER == 3:
                        hi_y(b, g)
                        hi_v(b, g)
                    for c in range(2, pieces(t)):
                        hi_pT(b, t, c)
                    for i in scored(t):
                        exp(b, i)
                with act.If(b < B - 1):
                    act.wait_ge(xn_stored, b * (16 * GROUPS) + 16 * GROUPS)
                    hi_xT(b, 0, 1)
                    hi_y(b, 0, 1)
                    for t in range(AHEAD):
                        exp(b, t, 1)
                    ln_rstd(b, GROUPS + 1)
                    hi_v(b, 0, 1)

            act.wait_ge(scales_loaded, 80)
            with act.Fori(0, CHUNKS // 2) as it:
                for u in range(2):
                    c = it * 2 + u
                    for n in range(3 * KH):
                        if n >= 4:
                            act.wait_ge(hid_ready, c * (3 * KH) + n - 3)
                        layer, j = divmod(n, KH)
                        if layer == 0:
                            act.wait_ge(pre_full, c * 32 + 2 * j + 1)
                            act.activation(act_out[:, n % 4], ps[:, 2 * (j % 2)], ACT.Silu,
                                           scale=scale_in[:, 0, j:j + 1]).then_inc(act_done, 1)
                        else:
                            act.wait_ge(pre_full, c * 32 + (2 + layer - 1) * KH + j + 1)
                            act.activation(act_out[:, n % 4], ps[:, j % 4], ACT.Gelu,
                                           scale=scale_hid[:, layer - 1, j:j + 1]).then_inc(act_done, 1)

        @block.vector
        def _(dve):
            def lo(dst, whole, hi, done):
                return dve.tensor_tensor(dst, whole, hi.bitcast(F32), ALU.subtract).then_inc(done, 1)

            def lo_weights(i, bank, scale):
                dve.wait_ge(proj_hi, i + 1)
                dve.scalar_tensor_tensor(
                    out=proj[:, i, 1].rearrange("p k n -> p (k n)"), in0=ps[:, bank], scalar=scale,
                    in1=proj[:, i, 0].rearrange("p k n -> p (k n)").bitcast(F32), op0=ALU.mult, op1=ALU.subtract
                ).then_inc(proj_ready, 1)

            def ln_moments(b, g):
                dve.wait_ge(x_loaded, b * (16 * GROUPS) + 16 * (g + 1))
                for r in range(PER):
                    last = dve.bn_stats(stats[:, r], xs[:, r])
                last.then_inc(stats_done, 1)
                at = b * (2 * GROUPS) + 2 * g
                dve.wait_ge(stats_done, b * GROUPS + g + 1)
                dve.tensor_tensor(halves[:, 0], stats[:, :, 1], stats[:, :, 4], ALU.add)
                dve.tensor_tensor(halves[:, 1], stats[:, :, 1], stats[:, :, 4], ALU.subtract)
                dve.tensor_tensor(halves[:, 2], stats[:, :, 2], stats[:, :, 5], ALU.add).then_inc(moment_step, 1)
                dve.wait_ge(moment_step, at + 1)
                dve.tensor_scalar(mean[:], halves[:, 0], 0.5, None, ALU.mult)
                dve.tensor_tensor(halves[:, 3], halves[:, 1], halves[:, 1], ALU.mult).then_inc(moment_step, 1)
                dve.wait_ge(moment_step, at + 2)
                dve.scalar_tensor_tensor(out=d_var[:], in0=halves[:, 3], scalar=D / 4, in1=halves[:, 2],
                                         op0=ALU.mult, op1=ALU.add).then_inc(moments_done, 1)

            def ln_apply(b, g):
                at = b * (3 * GROUPS) + 3 * g
                dve.wait_ge(rstd0_done, b * GROUPS + g + 1)
                dve.tensor_tensor(newton[:, 0], rstd0[:], rstd0[:], ALU.mult)
                dve.tensor_scalar(newton[:, 1], d_var[:], 1.0 / D, LN_EPS, ALU.mult, ALU.add)\
                   .then_inc(newton_step, 1)
                dve.wait_ge(newton_step, at + 1)
                dve.scalar_tensor_tensor(out=newton[:, 2], in0=newton[:, 0], scalar=-0.5, in1=newton[:, 1],
                                         op0=ALU.mult, op1=ALU.mult).then_inc(newton_step, 1)
                dve.wait_ge(newton_step, at + 2)
                dve.scalar_tensor_tensor(out=rstd[:], in0=newton[:, 2], scalar=1.5, in1=rstd0[:],
                                         op0=ALU.add, op1=ALU.mult).then_inc(newton_step, 1)
                dve.wait_ge(newton_step, at + 3)
                for r in range(PER):
                    last = dve.tensor_scalar(xs[:, r], xs[:, r], mean[:, r:r + 1], rstd[:, r:r + 1],
                                             ALU.subtract, ALU.mult)
                last.then_inc(xn_ready, 1)

            def lo_of(b, use, hi, dst, ahead):
                dve.wait_ge(misc_hi, misc_count(b, use, ahead))
                lo(dst, ps[:, misc_bank(use), 0:dst.shape[-1]], hi, misc_empty)

            def lo_xT(b, g, ahead=0):
                for k in range(KD):
                    lo_of(b, ("xT", g, k), xnT[:, g, 0, k], xnT[:, g, 1, k], ahead)

            def lo_y(b, g, ahead=0):
                for m in range(KD):
                    lo_of(b, ("y", g, m), yT[:, 0, m], yT[:, 1, m], ahead)

            def lo_v(b, g, ahead=0):
                for h in range(2):
                    use = ("v", g, h)
                    two = slice(g * PER + 2 * h, g * PER + 2 * h + 2)
                    dve.wait_ge(misc_hi, misc_count(b, use, ahead))
                    lo(val[:, two, 1], ps[:, misc_bank(use)].rearrange("p (t n) -> p t n", t=2),
                       val[:, two, 0], misc_empty)

            def lo_pT(b, t, c):
                slot, n = piece(t, c) % PT_SLOTS, width(t, c)
                lo_of(b, ("pT", t, c), probsT[:, slot, 0, 0:n], probsT[:, slot, 1, 0:n], 0)

            def row_max(b, t, ahead=0):
                n = pieces(t)
                for c in range(n):
                    dve.wait_ge(scores_full, b * PIECES + (ahead * PIECES + piece(t, c) + 1))
                    scores = ps[:, scores_at(t, c), 0:width(t, c)]
                    if n == 1:
                        dve.tensor_reduce(neg_max[:, t % PER:t % PER + 1], scores, X, ALU.max, negate=True)\
                           .then_inc(max_ready, 1)
                    else:
                        dve.tensor_reduce(piece_max[:, c:c + 1], scores, X, ALU.max)\
                           .then_inc(pieces_max_done, 1)
                if n > 1:
                    dve.wait_ge(pieces_max_done, b * (PIECES - PER) + piece(t) - PER + n)
                    dve.tensor_reduce(neg_max[:, t % PER:t % PER + 1], piece_max[:, 0:n], X, ALU.max, negate=True)\
                       .then_inc(max_ready, 1)

            def finish(b, t):
                n = pieces(t)
                at = b * (2 * TILES) + 2 * t
                dve.wait_ge(probs_ready, b * PIECES + piece(t, n))
                dve.tensor_reduce(row_sum[:], piece_sum[:, t % PER, 0:n], X, ALU.add).then_inc(norm_step, 1)
                dve.wait_ge(norm_step, at + 1)
                dve.reciprocal(row_inv[:], row_sum[:]).then_inc(norm_step, 1)
                dve.wait_ge(norm_step, at + 2)
                slot = t % RES_SLOTS
                dve.wait_ge(res_loaded[slot], b * (16 * PER) + 16 * (t // RES_SLOTS + 1))
                dve.wait_ge(out_full, b * PIECES + piece(t, n))
                dve.scalar_tensor_tensor(out=res[:, slot], in0=ps[:, OUT_BANK, 0:D], scalar=row_inv[:],
                                         in1=res[:, slot], op0=ALU.mult, op1=ALU.add).then_inc(out_evacuated, 1)

            ln_moments(0, 0)
            ln_apply(0, 0)
            lo_weights(0, A_BANK, float(D) ** -0.5)
            lo_xT(0, 0)
            lo_weights(1, OUT_BANK, 1.0)
            dve.memset(row_sum[:], 1.0).then_inc(out_evacuated, 1)
            lo_y(0, 0)
            for t in range(AHEAD):
                row_max(0, t)
            ln_moments(0, 1)
            lo_v(0, 0)
            with dve.Fori(0, B) as b:
                for t in range(TILES):
                    g = t // PER + 1
                    for i, c in transposed(t):
                        lo_pT(b, i, c)
                    if g < GROUPS and t % PER == 2:
                        lo_xT(b, g)
                    if g < GROUPS and t % PER == 3:
                        lo_y(b, g)
                        lo_v(b, g)
                    for i in scored(t):
                        row_max(b, i)
                    for c in range(2, pieces(t)):
                        lo_pT(b, t, c)
                    if t % PER == 0 and 1 < g < GROUPS:
                        ln_moments(b, g)
                    if t % PER == 1 and 1 < g < GROUPS:
                        ln_apply(b, g)
                    if g == GROUPS and t % PER < 2:
                        with dve.If(b < B - 1):
                            (ln_moments, ln_apply)[t % PER](b, GROUPS)
                    if t == TILES - 2:
                        with dve.If(b > B - 2):
                            dve.wait_ge(low_step, 2 + 3 * (WCOLS // CHECK))
                            dve.tensor_reduce(low_any[:], low_sum[:], X, ALU.max).then_inc(low_ready, 1)
                    if t == TILES - 1:
                        with dve.If(b < B - 1):
                            lo_xT(b, 0, 1)
                            lo_y(b, 0, 1)
                        with dve.Else():
                            dve.wait_ge(low_summed, 1)
                            dve.tensor_scalar(inexact[:], ps[0:1, 0, 0:1], 0.0, None, ALU.is_gt)\
                               .then_inc(inexact_ready, 1)
                    finish(b, t)
                    if t == 0:
                        ln_apply(b, 1)
                with dve.If(b < B - 1):
                    for t in range(AHEAD):
                        row_max(b, t, 1)
                    ln_moments(b, GROUPS + 1)
                    lo_v(b, 0, 1)

            dve.wait_ge(scales_loaded, 80)
            with dve.Fori(0, CHUNKS // 2) as it:
                for u in range(2):
                    c = it * 2 + u
                    for n in range(3 * KH):
                        layer, j = divmod(n, KH)
                        dst = hidden[(u + layer) % 2][:, j]
                        whole = act_out[:, n % 4]
                        dve.wait_ge(act_done, c * (3 * KH) + n + 1)
                        if layer == 0:
                            dve.wait_ge(pre_full, c * 32 + 2 * j + 2)
                            dve.scalar_tensor_tensor(out=gated[:, j % 2], in0=ps[:, 2 * (j % 2) + 1],
                                                     scalar=scale_in[:, 1, j:j + 1], in1=whole,
                                                     op0=ALU.mult, op1=ALU.mult).then_inc(gate_done, 1)
                            whole = gated[:, j % 2]
                            dve.wait_ge(gate_done, c * KH + j + 1)
                        dve.tensor_copy(dst[:, 0], whole).then_inc(hi_done, 1)
                        dve.wait_ge(hi_done, c * (3 * KH) + n + 1)
                        lo(dst[:, 1], whole, dst[:, 0], hid_ready)
                    dve.wait_ge(res_chunk_loaded, c * 16 + 16)
                    for r in range(PER):
                        dve.wait_ge(ffn_full, c * PER + r + 1)
                        dve.tensor_tensor(gated[:, r % 2, 0:D], ps[:, 4 + r, 0:D], scale_out[:], ALU.mult)\
                           .then_inc(ffn_scaled, 1)
                        dve.wait_ge(ffn_scaled, c * PER + r + 1)
                        dve.tensor_tensor(res[:, r], res[:, r], gated[:, r % 2, 0:D], ALU.add)\
                           .then_inc(out_evacuated, 1)

        @block.tensor
        def _(pe):
            PARTS = ((0, 0), (0, 1), (1, 0))

            def split_product(dst, lhs, rhs, start=True, stop=True):
                for k in range(KD):
                    for n, (p, q) in enumerate(PARTS):
                        mm = pe.matmul(dst, lhs(p, k), rhs(q, k), start=start and k == 0 and n == 0,
                                       stop=stop and k == KD - 1 and n == len(PARTS) - 1)
                return mm

            def take_bank(b, use, ahead=0):
                if use == SIDE_USE:
                    pe.wait_ge(out_evacuated, b * TILES + (ahead * TILES + 1))
                else:
                    n = RING.index(use)
                    if n >= len(MISC_BANKS):
                        pe.wait_ge(misc_empty, misc_count(b, RING[n - len(MISC_BANKS)], ahead))
                    elif ahead:
                        pe.wait_ge(misc_empty, misc_count(b, RING[n - len(MISC_BANKS)]))
                return ps[:, misc_bank(use)]

            def transpose_x(b, g, ahead=0):
                pe.wait_ge(xn_ready, b * GROUPS + (ahead * GROUPS + g + 1))
                for k in range(KD):
                    bank = take_bank(b, ("xT", g, k), ahead)
                    for r in range(PER):
                        mm = pe.transpose(bank[:, r * P:(r + 1) * P], xs[:, r, k * P:(k + 1) * P], ident[:])
                    mm.then_inc(misc_full, 1)

            def project_y(b, g, ahead=0):
                pe.wait_ge(misc_empty, misc_count(b, ("xT", g, KD - 1), ahead))
                for m in range(KD):
                    split_product(take_bank(b, ("y", g, m), ahead), lambda p, k: proj[:, 0, p, k, m * P:(m + 1) * P],
                                  lambda q, k: xnT[:, g, q, k]).then_inc(misc_full, 1)

            def project_v(b, g, ahead=0):
                for h in range(2):
                    bank = take_bank(b, ("v", g, h), ahead)
                    for i in range(2):
                        r = 2 * h + i
                        mm = split_product(bank[:, i * D:(i + 1) * D],
                                           lambda p, k: xnT[:, g, p, k, r * P:(r + 1) * P],
                                           lambda q, k: proj[:, 1, q, k])
                    mm.then_inc(misc_full, 1)

            def score(b, t, ahead=0):
                g, r = divmod(t, PER)
                if r == 0:
                    pe.wait_ge(misc_empty, misc_count(b, ("y", g, KD - 1), ahead))
                if ahead:
                    pe.wait_ge(probs_ready, b * PIECES + PIECES)
                for c in range(pieces(t)):
                    at, n = scores_at(t, c), width(t, c)
                    if last_at(t, c):
                        pe.wait_ge(probs_ready, b * PIECES + piece(*last_at(t, c)) + 1)
                    mm = split_product(ps[:, at, 0:n], lambda p, k: yT[:, p, k, r * P:(r + 1) * P],
                                       lambda q, k: xnT[:, c, q, k, 0:n], stop=c < g)
                    if c == g:
                        mm = pe.matmul(ps[:, at, r * P:(r + 1) * P], ident_h[:], mask[:], start=False, stop=True)
                    mm.then_inc(scores_full, 1)

            def transpose_probs(b, t, c):
                pe.wait_ge(probs_ready, b * PIECES + piece(t, c) + 1)
                bank, at = take_bank(b, ("pT", t, c)), scores_at(t, c) * BANK
                for i in range(width(t, c) // P):
                    mm = pe.transpose(bank[:, i * P:(i + 1) * P],
                                      probs[:, at + i * P:at + (i + 1) * P], ident[:])
                mm.then_inc(misc_full, 1)

            def attend(b, t, c):
                if c == 0:
                    pe.wait_ge(out_evacuated, b * TILES + t + 1)
                pe.wait_ge(misc_empty, misc_count(b, ("pT", t, c)))
                slot, n = piece(t, c) % PT_SLOTS, width(t, c) // P
                for i in range(n):
                    for j, (p, q) in enumerate(PARTS):
                        mm = pe.matmul(ps[:, OUT_BANK, 0:D], probsT[:, slot, p, i * P:(i + 1) * P],
                                       val[:, c * PER + i, q], start=(c == 0 and i == 0 and j == 0),
                                       stop=(c == pieces(t) - 1 and i == n - 1 and j == len(PARTS) - 1))
                mm.then_inc(out_full, 1)

            def multiply_weights(loaded, bank, lhs, rhs):
                pe.wait_ge(loaded, 32)
                for m in range(KD):
                    for k in range(KD):
                        mm = pe.matmul(ps[:, bank, m * D:(m + 1) * D], attn_w[:, lhs, k, m * P:(m + 1) * P],
                                       attn_w[:, rhs, k], start=(k == 0), stop=(k == KD - 1))
                mm.then_inc(proj_full, 1)

            pe.wait_ge(consts_ready, 4)
            for _ in range(WARM_UP):
                pe.matmul(ps[:, 0, 0:P], ident_h[:], mask[:], start=True, stop=True)
            multiply_weights(qk_loaded, A_BANK, 0, 1)
            transpose_x(0, 0)
            multiply_weights(vo_loaded, OUT_BANK, 2, 3)
            pe.wait_ge(proj_ready, 1)
            project_y(0, 0)
            for t in range(AHEAD):
                score(0, t)
            pe.wait_ge(proj_ready, 2)
            project_v(0, 0)
            with pe.Fori(0, B) as b:
                for t in range(TILES):
                    g, n = t // PER + 1, pieces(t)
                    for i, c in transposed(t):
                        transpose_probs(b, i, c)
                    if g < GROUPS and t % PER == 2:
                        transpose_x(b, g)
                    if g < GROUPS and t % PER == 3:
                        project_y(b, g)
                        project_v(b, g)
                    for i in scored(t):
                        score(b, i)
                    for c in range(n):
                        if c + 2 < n:
                            transpose_probs(b, t, c + 2)
                        attend(b, t, c)
                        if t == TILES - 1 and 0 < c < n - 1:
                            with pe.If(b < B - 1):
                                (transpose_x, project_y)[c - 1](b, 0, 1)
                            if c == n - 2:
                                with pe.Else():
                                    pe.wait_ge(low_ready, 1)
                                    pe.matmul(ps[0:1, 0, 0:1], low_any[:], ones[:], start=True, stop=True)\
                                      .then_inc(low_summed, 1)
                with pe.If(b < B - 1):
                    for t in range(AHEAD):
                        score(b, t, 1)
                    project_v(b, 0, 1)

            pe.wait_ge(inexact_ready, 1)
            some_low = pe.value_load(inexact[0:1, 0:1])

            def feed_forward(view):
                def layer_tile(dst, at, j, src, ks, ready=None):
                    for k in range(ks):
                        if ready is not None:
                            pe.wait_ge(hid_ready, ready + k + 1)
                        for p in range(2):
                            mm = pe.matmul(dst, view(weights[:, at + k * HID + j * P:at + k * HID + (j + 1) * P]),
                                           view(src(p, k)), start=(k == 0 and p == 0),
                                           stop=(k == ks - 1 and p == 1))
                    mm.then_inc(pre_full, 1)

                with pe.Fori(0, CHUNKS // 2) as it:
                    for u in range(2):
                        c = it * 2 + u
                        pe.wait_ge(chunk_loaded[u], it * 16 + 16)
                        for j in range(KH):
                            if j >= 2:
                                pe.wait_ge(gate_done, c * KH + j - 1)
                            for i, at in enumerate((W1, W2)):
                                layer_tile(ps[:, 2 * (j % 2) + i], at, j, lambda p, k: chunk_x[:, u, p, k], KD)
                        for layer, at in ((1, H1), (2, H2)):
                            src = hidden[(u + layer + 1) % 2]
                            for j in range(KH):
                                if layer == 1 and j < 4:
                                    pe.wait_ge(gate_done, c * KH + KH - 1 + j // 2)
                                else:
                                    pe.wait_ge(act_done, c * (3 * KH) + layer * KH + j - 3)
                                layer_tile(ps[:, j % 4], at, j, lambda p, k: src[:, k, p], KH,
                                           c * (3 * KH) + (layer - 1) * KH if j == 0 else None)
                        src = hidden[u]
                        pe.wait_ge(out_evacuated, c * PER + (B * TILES + 1))
                        half = KH // 2
                        steps = [(k, r) for k in range(half) for r in range(PER)]
                        steps += [(k, r) for r in range(PER) for k in range(half, KH)]
                        for k, r in steps:
                            if r == 0:
                                pe.wait_ge(hid_ready, c * (3 * KH) + 2 * KH + k + 1)
                            for p in range(2):
                                mm = pe.matmul(ps[:, 4 + r, 0:D], view(src[:, k, p, r * P:(r + 1) * P]),
                                               view(weights[:, W3 + k * D:W3 + (k + 1) * D]),
                                               start=(k == 0 and p == 0), stop=(k == KH - 1 and p == 1))
                            if k == KH - 1:
                                mm.then_inc(ffn_full, 1)

            with pe.If(some_low == 0):
                feed_forward(lambda a: a)
            with pe.Else():
                feed_forward(lambda a: a.bitcast(F32))


_FFN_W = ("L0_ffn_w1_w", "L0_ffn_w2_w", "L0_ffn_h1_w", "L0_ffn_h2_w", "L0_ffn_w3_w")
_SCALES = ("L0_ffn_w1_s", "L0_ffn_w2_s", "L0_ffn_h1_s", "L0_ffn_h2_s")


def kernel(**inputs):
    import numpy as np
    import concourse.bacc as bacc
    from concourse.bass_utils import run_bass_kernel_spmd

    arrays = {"x": np.asarray(inputs["L0_attn_x"])}
    for name in ("Wq", "Wk", "Wv"):
        arrays[name + "T"] = np.asarray(inputs["L0_attn_" + name]).T
    arrays["Wo"] = np.asarray(inputs["L0_attn_Wo"])
    tiles = [np.asarray(inputs[n]).T.reshape(-1, P, inputs[n].shape[0]).transpose(1, 0, 2).reshape(P, -1) for n in _FFN_W]
    arrays["ffn_w"] = np.concatenate(tiles, axis=1).reshape(P, LOADS, LOAD).transpose(1, 0, 2)
    for name in _SCALES:
        arrays[name] = np.asarray(inputs[name]).reshape(KH, P).T
    arrays["w3_s"] = np.asarray(inputs["L0_ffn_w3_s"])

    nc = bacc.Bacc("TRN2", target_bir_lowering=False, num_devices=1)
    arrays = {"in_" + n: np.ascontiguousarray(a) for n, a in arrays.items()}
    args = [nc.dram_tensor(n, a.shape, mybir.dt.from_np(a.dtype), kind="ExternalInput").ap() for n, a in arrays.items()]
    out = nc.dram_tensor("out_0", (B, S, D), F32, kind="ExternalOutput").ap()
    build(nc, *args, out)
    r = run_bass_kernel_spmd(nc, [arrays], core_ids=[0])
    return r.results[0]["out_0"]
```
